# Optimizing a Trainium2 kernel written in Bass

```python
import numpy as np
import jax
import jax.numpy as jnp

def _softmax(x, axis=-1):
    return jax.nn.softmax(x, axis=axis)

def _gelu(x):
    return jax.nn.gelu(x, approximate=True)

def _silu(x):
    return jax.nn.silu(x)

def _sigmoid(x):
    return jax.nn.sigmoid(x)

def _layernorm(x, axis=-1, eps=1e-05):
    m = jnp.mean(x, axis=axis, keepdims=True)
    v = jnp.var(x, axis=axis, keepdims=True)
    return (x - m) / jnp.sqrt(v + eps)

def _scatter_add(tgt, idx, src, axis=0):
    return tgt.at[idx].add(src)

def _segment_sum(src, seg, n):
    return jax.ops.segment_sum(src, seg, n)
kernel_name = 'mk_dlrm_tower_d1_rec_r8_4e91fe'

def setup_inputs(seed: int=0):
    np.random.seed(seed)
    _w = jnp.asarray

    def _rec_inputs():
        import jax
        import jax.numpy as jnp
        _tk = jax.random.key(seed)
        dense_ctx = jax.random.normal(jax.random.fold_in(_tk, 190), (512, 16), jnp.float32)
        ids = jnp.stack([jax.random.randint(jax.random.fold_in(_tk, 200 + f), (512,), 0, v, jnp.int32) for f, v in enumerate([125000, 1250, 1000, 1000, 1250, 12500, 12500, 1250, 1000, 1250, 1000, 1000, 1000, 12500, 12500, 1000, 1000, 1250, 12500, 125000, 1250, 1250, 12500, 12500, 125000, 1000, 1000, 1250, 12500, 125000, 1250, 1250, 12500, 125000, 125000, 12500, 125000, 125000, 1000])], axis=1)
        tbl_0 = 0.05 * jax.random.normal(jax.random.fold_in(_tk, 500 + 0), (125000, 16), jnp.float32)
        tbl_1 = 0.05 * jax.random.normal(jax.random.fold_in(_tk, 500 + 1), (1250, 16), jnp.float32)
        tbl_2 = 0.05 * jax.random.normal(jax.random.fold_in(_tk, 500 + 2), (1000, 16), jnp.float32)
        tbl_3 = 0.05 * jax.random.normal(jax.random.fold_in(_tk, 500 + 3), (1000, 16), jnp.float32)
        tbl_4 = 0.05 * jax.random.normal(jax.random.fold_in(_tk, 500 + 4), (1250, 16), jnp.float32)
        tbl_5 = 0.05 * jax.random.normal(jax.random.fold_in(_tk, 500 + 5), (12500, 16), jnp.float32)
        tbl_6 = 0.05 * jax.random.normal(jax.random.fold_in(_tk, 500 + 6), (12500, 16), jnp.float32)
        tbl_7 = 0.05 * jax.random.normal(jax.random.fold_in(_tk, 500 + 7), (1250, 16), jnp.float32)
        tbl_8 = 0.05 * jax.random.normal(jax.random.fold_in(_tk, 500 + 8), (1000, 16), jnp.float32)
        tbl_9 = 0.05 * jax.random.normal(jax.random.fold_in(_tk, 500 + 9), (1250, 16), jnp.float32)
        tbl_10 = 0.05 * jax.random.normal(jax.random.fold_in(_tk, 500 + 10), (1000, 16), jnp.float32)
        tbl_11 = 0.05 * jax.random.normal(jax.random.fold_in(_tk, 500 + 11), (1000, 16), jnp.float32)
        tbl_12 = 0.05 * jax.random.normal(jax.random.fold_in(_tk, 500 + 12), (1000, 16), jnp.float32)
        tbl_13 = 0.05 * jax.random.normal(jax.random.fold_in(_tk, 500 + 13), (12500, 16), jnp.float32)
        tbl_14 = 0.05 * jax.random.normal(jax.random.fold_in(_tk, 500 + 14), (12500, 16), jnp.float32)
        tbl_15 = 0.05 * jax.random.normal(jax.random.fold_in(_tk, 500 + 15), (1000, 16), jnp.float32)
        tbl_16 = 0.05 * jax.random.normal(jax.random.fold_in(_tk, 500 + 16), (1000, 16), jnp.float32)
        tbl_17 = 0.05 * jax.random.normal(jax.random.fold_in(_tk, 500 + 17), (1250, 16), jnp.float32)
        tbl_18 = 0.05 * jax.random.normal(jax.random.fold_in(_tk, 500 + 18), (12500, 16), jnp.float32)
        tbl_19 = 0.05 * jax.random.normal(jax.random.fold_in(_tk, 500 + 19), (125000, 16), jnp.float32)
        tbl_20 = 0.05 * jax.random.normal(jax.random.fold_in(_tk, 500 + 20), (1250, 16), jnp.float32)
        tbl_21 = 0.05 * jax.random.normal(jax.random.fold_in(_tk, 500 + 21), (1250, 16), jnp.float32)
        tbl_22 = 0.05 * jax.random.normal(jax.random.fold_in(_tk, 500 + 22), (12500, 16), jnp.float32)
        tbl_23 = 0.05 * jax.random.normal(jax.random.fold_in(_tk, 500 + 23), (12500, 16), jnp.float32)
        tbl_24 = 0.05 * jax.random.normal(jax.random.fold_in(_tk, 500 + 24), (125000, 16), jnp.float32)
        tbl_25 = 0.05 * jax.random.normal(jax.random.fold_in(_tk, 500 + 25), (1000, 16), jnp.float32)
        tbl_26 = 0.05 * jax.random.normal(jax.random.fold_in(_tk, 500 + 26), (1000, 16), jnp.float32)
        tbl_27 = 0.05 * jax.random.normal(jax.random.fold_in(_tk, 500 + 27), (1250, 16), jnp.float32)
        tbl_28 = 0.05 * jax.random.normal(jax.random.fold_in(_tk, 500 + 28), (12500, 16), jnp.float32)
        tbl_29 = 0.05 * jax.random.normal(jax.random.fold_in(_tk, 500 + 29), (125000, 16), jnp.float32)
        tbl_30 = 0.05 * jax.random.normal(jax.random.fold_in(_tk, 500 + 30), (1250, 16), jnp.float32)
        tbl_31 = 0.05 * jax.random.normal(jax.random.fold_in(_tk, 500 + 31), (1250, 16), jnp.float32)
        tbl_32 = 0.05 * jax.random.normal(jax.random.fold_in(_tk, 500 + 32), (12500, 16), jnp.float32)
        tbl_33 = 0.05 * jax.random.normal(jax.random.fold_in(_tk, 500 + 33), (125000, 16), jnp.float32)
        tbl_34 = 0.05 * jax.random.normal(jax.random.fold_in(_tk, 500 + 34), (125000, 16), jnp.float32)
        tbl_35 = 0.05 * jax.random.normal(jax.random.fold_in(_tk, 500 + 35), (12500, 16), jnp.float32)
        tbl_36 = 0.05 * jax.random.normal(jax.random.fold_in(_tk, 500 + 36), (125000, 16), jnp.float32)
        tbl_37 = 0.05 * jax.random.normal(jax.random.fold_in(_tk, 500 + 37), (125000, 16), jnp.float32)
        tbl_38 = 0.05 * jax.random.normal(jax.random.fold_in(_tk, 500 + 38), (1000, 16), jnp.float32)
        _rk = jax.random.fold_in(_tk, 7)
        W_top1 = 0.05 * jax.random.normal(jax.random.fold_in(_tk, 801), (400, 512), jnp.float32)
        W_top2 = 0.0441942 * jax.random.normal(jax.random.fold_in(_tk, 802), (512, 256), jnp.float32)
        W_top3 = 0.0625 * jax.random.normal(jax.random.fold_in(_tk, 803), (256, 1), jnp.float32)
        b_top1 = jnp.zeros((512,), jnp.float32)
        b_top2 = jnp.zeros((256,), jnp.float32)
        return (dense_ctx, ids, tbl_0, tbl_1, tbl_2, tbl_3, tbl_4, tbl_5, tbl_6, tbl_7, tbl_8, tbl_9, tbl_10, tbl_11, tbl_12, tbl_13, tbl_14, tbl_15, tbl_16, tbl_17, tbl_18, tbl_19, tbl_20, tbl_21, tbl_22, tbl_23, tbl_24, tbl_25, tbl_26, tbl_27, tbl_28, tbl_29, tbl_30, tbl_31, tbl_32, tbl_33, tbl_34, tbl_35, tbl_36, tbl_37, tbl_38, W_top1, b_top1, W_top2, b_top2, W_top3)
    dense_ctx, ids, tbl_0, tbl_1, tbl_2, tbl_3, tbl_4, tbl_5, tbl_6, tbl_7, tbl_8, tbl_9, tbl_10, tbl_11, tbl_12, tbl_13, tbl_14, tbl_15, tbl_16, tbl_17, tbl_18, tbl_19, tbl_20, tbl_21, tbl_22, tbl_23, tbl_24, tbl_25, tbl_26, tbl_27, tbl_28, tbl_29, tbl_30, tbl_31, tbl_32, tbl_33, tbl_34, tbl_35, tbl_36, tbl_37, tbl_38, W_top1, b_top1, W_top2, b_top2, W_top3 = _rec_inputs()

    def _L0_rec_setup():
        import jax, jax.numpy as jnp
        import numpy as np
        M_FIELDS = 39
        EMB_D = 16
        UNITS = [128, 128, 128]
        BATCH = 256

        def _cin_forward(x, ws, bs):
            b, m, D = x.shape
            prev = x
            logit = []
            for k in range(len(ws)):
                h = prev.shape[1]
                z = jnp.einsum('bmd,bhd->bdmh', x, prev).reshape(b, D, m * h)
                t = jnp.einsum('bdc,co->bdo', z, ws[k]) + bs[k]
                t = jnp.transpose(t, (0, 2, 1))
                norm = jnp.sqrt(jnp.sum(t * t, axis=(-2, -1), keepdims=True))
                t = t / norm
                logit.append(t)
                prev = t
            return jnp.sum(jnp.concatenate(logit, axis=1), axis=-1)
        key = jax.random.key(seed)
        ks = jax.random.split(key, 4)
        x = jax.random.normal(ks[0], (BATCH, M_FIELDS, EMB_D), dtype=jnp.float32)
        w0 = jax.random.normal(ks[1], (M_FIELDS * M_FIELDS, UNITS[0]), dtype=jnp.float32) * 0.05
        w1 = jax.random.normal(ks[2], (UNITS[0] * M_FIELDS, UNITS[1]), dtype=jnp.float32) * 0.05
        w2 = jax.random.normal(ks[3], (UNITS[1] * M_FIELDS, UNITS[2]), dtype=jnp.float32) * 0.05
        b0 = jnp.zeros((UNITS[0],), dtype=jnp.float32)
        b1 = jnp.zeros((UNITS[1],), dtype=jnp.float32)
        b2 = jnp.zeros((UNITS[2],), dtype=jnp.float32)
        return {'x': x, 'w0': w0, 'w1': w1, 'w2': w2, 'b0': b0, 'b1': b1, 'b2': b2}
    _L0_rec_all = _L0_rec_setup()
    _L0_rec_in = {k: v for k, v in _L0_rec_all.items() if k in ('w0', 'w1', 'w2', 'b0', 'b1', 'b2')}
    del _L0_rec_all
    return {'dense_ctx': dense_ctx, 'ids': ids, 'tbl_0': tbl_0, 'tbl_1': tbl_1, 'tbl_2': tbl_2, 'tbl_3': tbl_3, 'tbl_4': tbl_4, 'tbl_5': tbl_5, 'tbl_6': tbl_6, 'tbl_7': tbl_7, 'tbl_8': tbl_8, 'tbl_9': tbl_9, 'tbl_10': tbl_10, 'tbl_11': tbl_11, 'tbl_12': tbl_12, 'tbl_13': tbl_13, 'tbl_14': tbl_14, 'tbl_15': tbl_15, 'tbl_16': tbl_16, 'tbl_17': tbl_17, 'tbl_18': tbl_18, 'tbl_19': tbl_19, 'tbl_20': tbl_20, 'tbl_21': tbl_21, 'tbl_22': tbl_22, 'tbl_23': tbl_23, 'tbl_24': tbl_24, 'tbl_25': tbl_25, 'tbl_26': tbl_26, 'tbl_27': tbl_27, 'tbl_28': tbl_28, 'tbl_29': tbl_29, 'tbl_30': tbl_30, 'tbl_31': tbl_31, 'tbl_32': tbl_32, 'tbl_33': tbl_33, 'tbl_34': tbl_34, 'tbl_35': tbl_35, 'tbl_36': tbl_36, 'tbl_37': tbl_37, 'tbl_38': tbl_38, 'W_top1': W_top1, 'b_top1': b_top1, 'W_top2': W_top2, 'b_top2': b_top2, 'W_top3': W_top3, 'L0_rec_w0': _L0_rec_in['w0'], 'L0_rec_w1': _L0_rec_in['w1'], 'L0_rec_w2': _L0_rec_in['w2'], 'L0_rec_b0': _L0_rec_in['b0'], 'L0_rec_b1': _L0_rec_in['b1'], 'L0_rec_b2': _L0_rec_in['b2']}

def reference(dense_ctx, ids, tbl_0, tbl_1, tbl_2, tbl_3, tbl_4, tbl_5, tbl_6, tbl_7, tbl_8, tbl_9, tbl_10, tbl_11, tbl_12, tbl_13, tbl_14, tbl_15, tbl_16, tbl_17, tbl_18, tbl_19, tbl_20, tbl_21, tbl_22, tbl_23, tbl_24, tbl_25, tbl_26, tbl_27, tbl_28, tbl_29, tbl_30, tbl_31, tbl_32, tbl_33, tbl_34, tbl_35, tbl_36, tbl_37, tbl_38, W_top1, b_top1, W_top2, b_top2, W_top3, L0_rec_w0, L0_rec_w1, L0_rec_w2, L0_rec_b0, L0_rec_b1, L0_rec_b2):
    import jax
    import jax.numpy as jnp

    def _L0_rec_ref(x, w0, w1, w2, b0, b1, b2):
        import jax, jax.numpy as jnp
        import numpy as np
        M_FIELDS = 39
        EMB_D = 16
        UNITS = [128, 128, 128]
        BATCH = 256

        def _cin_forward(x, ws, bs):
            b, m, D = x.shape
            prev = x
            logit = []
            for k in range(len(ws)):
                h = prev.shape[1]
                z = jnp.einsum('bmd,bhd->bdmh', x, prev).reshape(b, D, m * h)
                t = jnp.einsum('bdc,co->bdo', z, ws[k]) + bs[k]
                t = jnp.transpose(t, (0, 2, 1))
                norm = jnp.sqrt(jnp.sum(t * t, axis=(-2, -1), keepdims=True))
                t = t / norm
                logit.append(t)
                prev = t
            return jnp.sum(jnp.concatenate(logit, axis=1), axis=-1)
        return _cin_forward(x, [w0, w1, w2], [b0, b1, b2])
    e = jnp.stack([tbl_0[ids[:, 0]], tbl_1[ids[:, 1]], tbl_2[ids[:, 2]], tbl_3[ids[:, 3]], tbl_4[ids[:, 4]], tbl_5[ids[:, 5]], tbl_6[ids[:, 6]], tbl_7[ids[:, 7]], tbl_8[ids[:, 8]], tbl_9[ids[:, 9]], tbl_10[ids[:, 10]], tbl_11[ids[:, 11]], tbl_12[ids[:, 12]], tbl_13[ids[:, 13]], tbl_14[ids[:, 14]], tbl_15[ids[:, 15]], tbl_16[ids[:, 16]], tbl_17[ids[:, 17]], tbl_18[ids[:, 18]], tbl_19[ids[:, 19]], tbl_20[ids[:, 20]], tbl_21[ids[:, 21]], tbl_22[ids[:, 22]], tbl_23[ids[:, 23]], tbl_24[ids[:, 24]], tbl_25[ids[:, 25]], tbl_26[ids[:, 26]], tbl_27[ids[:, 27]], tbl_28[ids[:, 28]], tbl_29[ids[:, 29]], tbl_30[ids[:, 30]], tbl_31[ids[:, 31]], tbl_32[ids[:, 32]], tbl_33[ids[:, 33]], tbl_34[ids[:, 34]], tbl_35[ids[:, 35]], tbl_36[ids[:, 36]], tbl_37[ids[:, 37]], tbl_38[ids[:, 38]]], axis=1)
    z = _L0_rec_ref(e, L0_rec_w0, L0_rec_w1, L0_rec_w2, L0_rec_b0, L0_rec_b1, L0_rec_b2)
    z = z.reshape(z.shape[0], -1)
    h = jnp.concatenate([z, dense_ctx], axis=1)
    h = jnp.maximum(h @ W_top1 + b_top1, 0.0)
    h = jnp.maximum(h @ W_top2 + b_top2, 0.0)
    y = h @ W_top3
    return y

_drawn_inputs = setup_inputs


def setup_inputs(seed=0):
    import zlib

    import numpy as np

    out = dict(_drawn_inputs(seed))
    spreads = {'b_top1': (0.0, 0.1),
     'b_top2': (0.0, 0.1),
     'L0_rec_b0': (0.0, 0.1),
     'L0_rec_b1': (0.0, 0.1),
     'L0_rec_b2': (0.0, 0.1)}
    factors = {'tbl_0': 8.0,
     'tbl_1': 8.0,
     'tbl_2': 8.0,
     'tbl_3': 8.0,
     'tbl_4': 8.0,
     'tbl_5': 8.0,
     'tbl_6': 8.0,
     'tbl_7': 8.0,
     'tbl_8': 8.0,
     'tbl_9': 8.0,
     'tbl_10': 8.0,
     'tbl_11': 8.0,
     'tbl_12': 8.0,
     'tbl_13': 8.0,
     'tbl_14': 8.0,
     'tbl_15': 8.0,
     'tbl_16': 8.0,
     'tbl_17': 8.0,
     'tbl_18': 8.0,
     'tbl_19': 8.0,
     'tbl_20': 8.0,
     'tbl_21': 8.0,
     'tbl_22': 8.0,
     'tbl_23': 8.0,
     'tbl_24': 8.0,
     'tbl_25': 8.0,
     'tbl_26': 8.0,
     'tbl_27': 8.0,
     'tbl_28': 8.0,
     'tbl_29': 8.0,
     'tbl_30': 8.0,
     'tbl_31': 8.0,
     'tbl_32': 8.0,
     'tbl_33': 8.0,
     'tbl_34': 8.0,
     'tbl_35': 8.0,
     'tbl_36': 8.0,
     'tbl_37': 8.0,
     'tbl_38': 8.0,
     'L0_rec_w0': 5.899,
     'L0_rec_w1': 8.0,
     'L0_rec_w2': 8.0}
    for name, (base, spread) in spreads.items():
        noise = np.random.default_rng([zlib.crc32(name.encode()), seed]).standard_normal(out[name].shape)
        drawn = base * np.exp(spread * noise) if base else spread * noise
        out[name] = jnp.asarray(drawn.astype(out[name].dtype))
    for name, factor in factors.items():
        out[name] = (out[name] * factor).astype(out[name].dtype)
    return out
```

```python
from contextlib import ExitStack

import concourse.bass as bass
from concourse import mybir

ALU = mybir.AluOpType
ACT = mybir.ActivationFunctionType
F32 = mybir.dt.float32
I32 = mybir.dt.int32
AX_X = mybir.AxisListType.X

P = 128
BATCH = 512
FIELDS = 39
EMB = 16
UNITS = 128
LAYERS = 3
TILE_B = 32
TILES = BATCH // TILE_B
N = TILE_B * EMB

GROUP = P // TILE_B
GROUPS = -(-FIELDS // GROUP)
LAST_GROUP = FIELDS - GROUP * (GROUPS - 1)

SHIFTS = FIELDS // 2 + 1
PER_STEP = 3
STEPS0 = -(-SHIFTS // PER_STEP)
SHIFT_OF = [[PER_STEP * k + j + 1 for j in range(PER_STEP)] for k in range(STEPS0 - 1)] + [[SHIFTS - 1, 0]]
WIDE = PER_STEP * FIELDS
NARROW = 2 * FIELDS
XT_ROWS = FIELDS + SHIFTS - 1

CH = 3
CHUNKS = FIELDS // CH
ZSLOTS = 4

TOP1, TOP2 = 512, 256
DENSE = 16


def build(nc, ids_in, base_in, table, xt, dense_t, w0a, w0b, w1, w2, b0, b1, b2,
          wt1, bt1, wt2, bt2, wt3, out):
    ctx = ExitStack()
    with ctx:
        def sb(name, shape, dt=F32):
            return ctx.enter_context(nc.sbuf_tensor(name, shape, dt))

        def pb(name):
            return ctx.enter_context(nc.psum_tensor(name, [P, N], F32))

        def sem(name):
            return ctx.enter_context(nc.semaphore(name))

        ids_sb = sb("ids_sb", [P, TILES * GROUPS], I32)
        base_sb = sb("base_sb", [P, GROUPS], I32)
        rows_of = sb("rows_of", [P, GROUPS], I32)
        gathered = sb("gathered", [P, GROUPS, EMB])
        x3 = sb("x3", [WIDE, N])
        xr = sb("xr", [WIDE, STEPS0, N])
        z0 = sb("z0", [WIDE, STEPS0, N])
        xb = sb("xb", [P, FIELDS, N])
        z = sb("z", [P, ZSLOTS, CH, N])
        w0_sb = sb("w0_sb", [WIDE, STEPS0, UNITS])
        w0m = sb("w0m", [WIDE, STEPS0, UNITS])
        w_sb = [None, sb("w1_sb", [P, FIELDS, UNITS]), sb("w2_sb", [P, FIELDS, UNITS])]
        bias = sb("bias", [P, LAYERS])
        ones = sb("ones", [P, P])
        traw = sb("traw", [P, LAYERS, N])
        sq = sb("sq", [P, LAYERS, N])
        ssum = sb("ssum", [P, LAYERS, TILE_B])
        dsum = sb("dsum", [P, LAYERS, TILE_B])
        root = sb("root", [P, LAYERS, TILE_B])
        inv = sb("inv", [P, LAYERS, TILE_B])
        prod = sb("prod", [P, LAYERS, TILE_B])
        half = sb("half", [P, LAYERS, TILE_B])
        rnorm = sb("rnorm", [P, LAYERS, TILE_B])
        feat = sb("feat", [P, LAYERS, BATCH])
        dense_sb = sb("dense_sb", [DENSE, BATCH])
        bt1_sb = sb("bt1_sb", [P, TOP1 // P])
        bt2_sb = sb("bt2_sb", [P, TOP2 // P])
        wt3_sb = sb("wt3_sb", [P, TOP2 // P])
        top = xb[:, :, :].rearrange("p m n -> p (m n)")
        wt1_sb = top[:, 0:LAYERS * TOP1].rearrange("p (k o) -> p k o", k=LAYERS)
        wt1d_sb = top[0:DENSE, LAYERS * TOP1:4 * TOP1]
        wt2_sb = top[:, 4 * TOP1:4 * TOP1 + 4 * TOP2].rearrange("p (k o) -> p k o", k=4)
        h1 = z[:, 0:2, :, :].rearrange("p a b n -> p (a b n)")[:, 0:4 * BATCH].rearrange("p (k b) -> p k b", k=4)
        h2 = z[:, 2, 0:2, :]
        y_sb = traw[0:1, 0, :]

        acc = [pb(f"acc{k}") for k in range(LAYERS)]
        t_ps = [pb("t0_ps"), pb("t1_ps")]
        nrm = [pb(f"nrm{k}") for k in range(LAYERS)]

        ids_loaded = sem("ids_loaded")
        rows_ready, rows_seen = sem("rows_ready"), sem("rows_seen")
        rows_gathered = sem("rows_gathered")
        xt_written = sem("xt_written")
        w0a_loaded, w0b_loaded = sem("w0a_loaded"), sem("w0b_loaded")
        w_loaded = [None, sem("w1_loaded"), sem("w2_loaded")]
        small_loaded = sem("small_loaded")
        w0_ready = sem("w0_ready")
        ones_ready = sem("ones_ready")
        x0_loaded = sem("x0_loaded")
        xb_loaded = [sem(f"xb_loaded{c}") for c in range(CHUNKS)]
        z0_ready = sem("z0_ready")
        z_ready = sem("z_ready")
        z_used = sem("z_used")
        acc0_ready = sem("acc0_ready")
        raw_ready = [sem(f"raw_ready{k}") for k in range(LAYERS)]
        ssum_ready = [sem(f"ssum_ready{k}") for k in range(LAYERS)]
        nrm_ready = [sem(f"nrm_ready{k}") for k in range(LAYERS)]
        root_ready = [sem(f"root_ready{k}") for k in range(LAYERS)]
        step_done = sem("step_done")
        rnorm_ready = [sem(f"rnorm_ready{k}") for k in range(LAYERS)]
        t_ready = [sem("t0_ready"), sem("t1_ready")]
        feat_ready = [sem(f"feat_ready{k}") for k in range(LAYERS)]
        top_loaded = sem("top_loaded")
        h1_acc, h1_ready = sem("h1_acc"), sem("h1_ready")
        h2_acc, h2_ready = sem("h2_acc"), sem("h2_ready")
        y_acc, y_ready, y_written = sem("y_acc"), sem("y_ready"), sem("y_written")

        ZSTEPS = 2 * CHUNKS

        def slot_free(i, s):
            if s >= ZSLOTS:
                return ZSTEPS * i + s - ZSLOTS + 1
            last = max(r for r in range(ZSTEPS) if r % ZSLOTS == s)
            return None if isinstance(i, int) and i == 0 else ZSTEPS * (i - 1) + last + 1

        block = ctx.enter_context(nc.Block())

        @block.gpsimd
        def _(pool):
            nc.gpsimd.memset(ones[:, :], 1.0).then_inc(ones_ready, 1)
            pool.wait_ge(ids_loaded, 32)

            def gather(i):
                nc.gpsimd.tensor_tensor(rows_of[:, :], ids_sb[:, bass.ts(i, GROUPS)], base_sb[:, :],
                                        ALU.add).then_inc(rows_ready, 1)
                pool.wait_ge(rows_ready, i + 1)
                pool.sem_inc(rows_seen, 1)
                for g in range(GROUPS):
                    n = P if g < GROUPS - 1 else LAST_GROUP * TILE_B
                    nc.gpsimd.indirect_dma_start(
                        gathered[0:n, g, :], None, table[:, :],
                        bass.IndirectOffsetOnAxis(rows_of[0:n, g:g + 1], 0)).then_inc(rows_gathered, 16)
                pool.wait_ge(rows_gathered, 16 * GROUPS * (i + 1))
                for first, rows in ((0, FIELDS), (FIELDS, SHIFTS - 1)):
                    full, rest = divmod(rows, GROUP)
                    blk = xt[bass.ds(i, 1), first:first + rows, :].rearrange("a m n -> (a m) n")
                    pool.dma_start(blk[0:full * GROUP, :].rearrange("(g f) (b d) -> (f b) g d", f=GROUP, d=EMB),
                                   gathered[:, 0:full, :]).then_inc(xt_written, 16)
                    pool.dma_start(blk[full * GROUP:rows, :].rearrange("f (b d) -> (f b) d", d=EMB),
                                   gathered[0:rest * TILE_B, full, :]).then_inc(xt_written, 16)
                pool.wait_ge(xt_written, 64 * (i + 1))

            with pool.Fori(0, TILES) as i:
                gather(i)

        @block.sync
        def _(sp):
            sp.dma_start(ids_sb[:, :], ids_in).then_inc(ids_loaded, 16)
            sp.dma_start(base_sb[:, :], base_in).then_inc(ids_loaded, 16)
            sp.dma_start(w0m[:, :, :], w0b).then_inc(w0b_loaded, 16)
            sp.dma_start(w0_sb[:, :, :], w0a).then_inc(w0a_loaded, 16)

            def load_layer0(i):
                sp.wait_ge(xt_written, 64 * (i + 1))
                blk = xt[bass.ds(i, 1), :, :].rearrange("a m n -> (a m) n")
                for j in range(PER_STEP):
                    sp.dma_start(x3[j * FIELDS:(j + 1) * FIELDS, :], blk[0:FIELDS, :]).then_inc(x0_loaded, 16)
                    src = bass.AP(blk.tensor, blk.offset + (j + 1) * N,
                                  [[N, FIELDS], [PER_STEP * N, STEPS0 - 1], [1, N]])
                    sp.dma_start(xr[j * FIELDS:(j + 1) * FIELDS, 0:STEPS0 - 1, :], src).then_inc(x0_loaded, 16)
                for j, s in enumerate(SHIFT_OF[-1]):
                    sp.dma_start(xr[j * FIELDS:(j + 1) * FIELDS, STEPS0 - 1, :],
                                 blk[s:s + FIELDS, :]).then_inc(x0_loaded, 16)

            def load_fields(i):
                later = not (isinstance(i, int) and i == 0)
                for c in range(CHUNKS):
                    if later:
                        sp.wait_ge(z_ready, ZSTEPS * (i - 1) + CHUNKS + c + 1)
                    blk = xt[bass.ds(i, 1), c * CH:(c + 1) * CH, :].rearrange("a m n -> a (m n)")
                    sp.dma_start(xb[:, c * CH:(c + 1) * CH, :].rearrange("p m n -> p (m n)"),
                                 bass.AP(blk.tensor, blk.offset, [[0, P], [1, CH * N]])).then_inc(xb_loaded[c], 16)

            load_layer0(0)
            load_fields(0)
            sp.wait_ge(z0_ready, STEPS0)
            load_layer0(1)
            with sp.Fori(1, TILES - 1) as i:
                load_fields(i)
                load_layer0(i + 1)
            load_fields(TILES - 1)
            sp.wait_ge(z_ready, ZSTEPS * TILES)
            sp.dma_start(wt1_sb, wt1[0:LAYERS * P, :].rearrange("(k p) o -> p k o", p=P)).then_inc(top_loaded, 16)
            sp.dma_start(wt1d_sb, wt1[LAYERS * P:LAYERS * P + DENSE, :]).then_inc(top_loaded, 16)
            sp.dma_start(wt2_sb, wt2.rearrange("(k p) o -> p k o", p=P)).then_inc(top_loaded, 16)
            sp.wait_ge(y_ready, 1)
            sp.dma_start(out.rearrange("b a -> a b"), y_sb).then_inc(y_written, 16)
            sp.wait_ge(y_written, 16)

        @block.scalar
        def _(act):
            for k, b in enumerate((b0, b1, b2)):
                act.dma_start(bias[:, k:k + 1], b.rearrange("(p a) -> p a", a=1)).then_inc(small_loaded, 16)
            act.dma_start(w_sb[1][:, :, :], w1.rearrange("(m h) o -> h m o", h=P)).then_inc(w_loaded[1], 16)
            act.dma_start(w_sb[2][:, :, :], w2.rearrange("(m h) o -> h m o", h=P)).then_inc(w_loaded[2], 16)
            act.dma_start(dense_sb[:, :], dense_t).then_inc(small_loaded, 16)
            act.dma_start(bt1_sb[:, :], bt1.rearrange("(k p) -> p k", p=P),
                          allow_slow_non_contiguous=True).then_inc(small_loaded, 16)
            act.dma_start(bt2_sb[:, :], bt2.rearrange("(k p) -> p k", p=P),
                          allow_slow_non_contiguous=True).then_inc(small_loaded, 16)
            act.dma_start(wt3_sb[:, :], wt3.rearrange("(k p) a -> p (k a)", p=P),
                          allow_slow_non_contiguous=True).then_inc(small_loaded, 16)
            act.wait_ge(small_loaded, 7 * 16)

            def evacuate(k, i):
                if k == 0:
                    act.wait_ge(acc0_ready, i + 1)
                else:
                    act.wait_ge(z_used, ZSTEPS * i + k * CHUNKS)
                if not (isinstance(i, int) and i == 0):
                    act.wait_ge(feat_ready[k], i)
                nc.scalar.activation(sq[:, k, :], acc[k][:, :], ACT.Square,
                                     bias=bias[:, k:k + 1]).then_inc(raw_ready[k], 1)
                nc.scalar.activation(traw[:, k, :], acc[k][:, :], ACT.Identity,
                                     bias=bias[:, k:k + 1]).then_inc(raw_ready[k], 1)

            def square_root(k, i):
                act.wait_ge(nrm_ready[k], i + 1)
                nc.scalar.activation(root[:, k, :], nrm[k][:, 0:TILE_B], ACT.Sqrt).then_inc(root_ready[k], 1)

            def tile(i, first=False, last=False):
                if not first:
                    evacuate(2, i - 1)
                    square_root(2, i - 1)
                evacuate(1, i)
                square_root(1, i)
                if not last:
                    evacuate(0, i + 1)
                    square_root(0, i + 1)

            evacuate(0, 0)
            square_root(0, 0)
            tile(0, first=True)
            with act.Fori(1, TILES - 1) as i:
                tile(i)
            tile(TILES - 1, last=True)
            evacuate(2, TILES - 1)
            square_root(2, TILES - 1)

            for j in range(TOP1 // P):
                act.wait_ge(h1_acc, j + 1)
                nc.scalar.activation(h1[:, j, :], acc[j % 3][:, :], ACT.Relu,
                                     bias=bt1_sb[:, j:j + 1]).then_inc(h1_ready, 1)
            for j in range(TOP2 // P):
                act.wait_ge(h2_acc, j + 1)
                nc.scalar.activation(h2[:, j, :], t_ps[j][:, :], ACT.Relu,
                                     bias=bt2_sb[:, j:j + 1]).then_inc(h2_ready, 1)
            act.wait_ge(y_acc, 1)
            nc.scalar.copy(y_sb, nrm[0][0:1, :]).then_inc(y_ready, 1)

        @block.vector
        def _(dve):
            done = [0]

            def fields_of(k, c):
                return t_ps[k - 1][:, :].rearrange("p (a n) -> p a n", a=1).broadcast_to([P, CH, N])

            def products0(i):
                dve.wait_ge(x0_loaded, 16 * 8 * (i + 1))
                if not (isinstance(i, int) and i == 0):
                    dve.wait_ge(acc0_ready, i)
                for k in range(STEPS0):
                    n = WIDE if k < STEPS0 - 1 else NARROW
                    nc.vector.tensor_tensor(z0[0:n, k, :], x3[0:n, :], xr[0:n, k, :],
                                            ALU.mult).then_inc(z0_ready, 1)

            def products(i, k, c):
                s = (k - 1) * CHUNKS + c
                if c == 0:
                    dve.wait_ge(t_ready[k - 1], i + 1)
                if k == 1:
                    dve.wait_ge(xb_loaded[c], 16 * (i + 1))
                n = slot_free(i, s)
                if n is not None:
                    dve.wait_ge(z_used, n)
                nc.vector.tensor_tensor(
                    z[:, s % ZSLOTS, :, :], fields_of(k, c), xb[:, c * CH:(c + 1) * CH, :],
                    ALU.mult).then_inc(z_ready, 1)

            def sum_squares(k, i):
                dve.wait_ge(raw_ready[k], 2 * (i + 1))
                if not (isinstance(i, int) and i == 0):
                    dve.wait_ge(nrm_ready[k], i)
                nc.vector.tensor_reduce(ssum[:, k, :], sq[:, k, :].rearrange("p (b d) -> p b d", d=EMB),
                                        axis=AX_X, op=ALU.add).then_inc(ssum_ready[k], 1)
                nc.vector.tensor_reduce(dsum[:, k, :], traw[:, k, :].rearrange("p (b d) -> p b d", d=EMB),
                                        axis=AX_X, op=ALU.add).then_inc(step_done, 1)

            def normalize(k, i, order):
                base = 5 * order
                dve.wait_ge(root_ready[k], i + 1)
                total = nrm[k][:, 0:TILE_B]
                nc.vector.reciprocal(inv[:, k, :], root[:, k, :]).then_inc(step_done, 1)
                dve.wait_ge(step_done, base + 2)
                nc.vector.tensor_tensor(prod[:, k, :], total, inv[:, k, :], ALU.mult).then_inc(step_done, 1)
                dve.wait_ge(step_done, base + 3)
                nc.vector.scalar_tensor_tensor(half[:, k, :], prod[:, k, :], -0.5, inv[:, k, :],
                                               ALU.mult, ALU.mult).then_inc(step_done, 1)
                dve.wait_ge(step_done, base + 4)
                nc.vector.scalar_tensor_tensor(rnorm[:, k, :], half[:, k, :], 1.5, inv[:, k, :],
                                               ALU.add, ALU.mult).then_inc(step_done, 1)
                dve.wait_ge(step_done, base + 5)
                if k < 2:
                    nc.vector.tensor_tensor(
                        t_ps[k][:, :].rearrange("p (b d) -> p b d", d=EMB),
                        traw[:, k, :].rearrange("p (b d) -> p b d", d=EMB),
                        rnorm[:, k, :].rearrange("p (b a) -> p b a", a=1).broadcast_to([P, TILE_B, EMB]),
                        ALU.mult).then_inc(t_ready[k], 1)
                nc.vector.tensor_tensor(feat[:, k, bass.ts(i, TILE_B)], dsum[:, k, :], rnorm[:, k, :],
                                        ALU.mult).then_inc(feat_ready[k], 1)

            def tile(i, first=False, last=False):
                for c in range(CHUNKS):
                    products(i, 1, c)
                    if c == 3 and not first:
                        sum_squares(2, i - 1)
                    if c == 6 and not first:
                        normalize(2, i - 1, 3 * i)
                if not last:
                    products0(i + 1)
                sum_squares(1, i)
                normalize(1, i, 3 * i + 1)
                for c in range(CHUNKS):
                    products(i, 2, c)
                    if c == 3 and not last:
                        sum_squares(0, i + 1)
                    if c == 6 and not last:
                        normalize(0, i + 1, 3 * i + 2)

            dve.wait_ge(w0a_loaded, 16)
            dve.wait_ge(w0b_loaded, 16)
            nc.vector.tensor_tensor(w0_sb[:, 0:STEPS0 - 1, :], w0_sb[:, 0:STEPS0 - 1, :],
                                    w0m[:, 0:STEPS0 - 1, :], ALU.add).then_inc(w0_ready, 1)
            nc.vector.tensor_tensor(w0_sb[0:FIELDS, STEPS0 - 1, :], w0_sb[0:FIELDS, STEPS0 - 1, :],
                                    w0m[0:FIELDS, STEPS0 - 1, :], ALU.add).then_inc(w0_ready, 1)
            products0(0)
            sum_squares(0, 0)
            normalize(0, 0, 0)
            tile(0, first=True)
            with dve.Fori(1, TILES - 1) as i:
                tile(i)
            tile(TILES - 1, last=True)
            sum_squares(2, TILES - 1)
            normalize(2, TILES - 1, 3 * TILES - 1 + 0)

        @block.tensor
        def _(pe):
            def layer0(i, parts):
                for k in parts:
                    if k == 0 and not (isinstance(i, int) and i == 0):
                        pe.wait_ge(raw_ready[0], 2 * i)
                    n = WIDE if k < STEPS0 - 1 else NARROW
                    pe.wait_ge(z0_ready, STEPS0 * i + k + 1)
                    last = nc.tensor.matmul(acc[0][:, :], w0_sb[0:n, k, :], z0[0:n, k, :],
                                            start=(k == 0), stop=(k == STEPS0 - 1))
                if parts[-1] == STEPS0 - 1:
                    last.then_inc(acc0_ready, 1)

            def layer(i, k, chunks):
                for c in chunks:
                    if c == 0 and not (isinstance(i, int) and i == 0):
                        pe.wait_ge(raw_ready[k], 2 * i)
                    s = (k - 1) * CHUNKS + c
                    pe.wait_ge(z_ready, ZSTEPS * i + s + 1)
                    for r in range(CH):
                        m = CH * c + r
                        last = nc.tensor.matmul(acc[k][:, :], w_sb[k][:, m, :], z[:, s % ZSLOTS, r, :],
                                                start=(m == 0), stop=(m == FIELDS - 1))
                    last.then_inc(z_used, 1)

            def add_partitions(k, i):
                pe.wait_ge(ssum_ready[k], i + 1)
                if not (isinstance(i, int) and i == 0):
                    pe.wait_ge(feat_ready[k], i)
                nc.tensor.matmul(nrm[k][:, 0:TILE_B], ones[:, :], ssum[:, k, :],
                                 start=True, stop=True).then_inc(nrm_ready[k], 1)

            def tile(i, first=False, last=False):
                layer(i, 1, range(0, 4))
                if not first:
                    add_partitions(2, i - 1)
                layer(i, 1, range(4, CHUNKS))
                if not last:
                    layer0(i + 1, range(0, 4))
                add_partitions(1, i)
                if not last:
                    layer0(i + 1, range(4, STEPS0))
                layer(i, 2, range(0, 4))
                if not last:
                    add_partitions(0, i + 1)
                layer(i, 2, range(4, CHUNKS))

            pe.wait_ge(w0_ready, 2)
            pe.wait_ge(ones_ready, 1)
            layer0(0, range(STEPS0))
            add_partitions(0, 0)
            for k in (1, 2):
                pe.wait_ge(w_loaded[k], 16)
            tile(0, first=True)
            with pe.Fori(1, TILES - 1) as i:
                tile(i)
            tile(TILES - 1, last=True)
            add_partitions(2, TILES - 1)

            pe.wait_ge(top_loaded, 48)
            pe.wait_ge(small_loaded, 7 * 16)
            pe.wait_ge(feat_ready[2], TILES)
            for j in range(TOP1 // P):
                if j == 3:
                    pe.wait_ge(h1_ready, 1)
                o = slice(j * P, (j + 1) * P)
                for k in range(LAYERS):
                    nc.tensor.matmul(acc[j % 3][:, :], wt1_sb[:, k, o], feat[:, k, :], start=(k == 0), stop=False)
                nc.tensor.matmul(acc[j % 3][:, :], wt1d_sb[:, o], dense_sb[:, :],
                                 start=False, stop=True).then_inc(h1_acc, 1)
            for j in range(TOP2 // P):
                for k in range(TOP1 // P):
                    pe.wait_ge(h1_ready, k + 1)
                    last = nc.tensor.matmul(t_ps[j][:, :], wt2_sb[:, k, j * P:(j + 1) * P], h1[:, k, :],
                                            start=(k == 0), stop=(k == TOP1 // P - 1))
                last.then_inc(h2_acc, 1)
            for k in range(TOP2 // P):
                pe.wait_ge(h2_ready, k + 1)
                last = nc.tensor.matmul(nrm[0][0:1, :], wt3_sb[:, k:k + 1], h2[:, k, :],
                                        start=(k == 0), stop=(k == TOP2 // P - 1))
            last.then_inc(y_acc, 1)


def kernel(**inputs):
    import numpy as np
    import concourse.bacc as bacc
    from concourse import mybir as mb
    from concourse.bass_utils import run_bass_kernel_spmd as run

    a = {name: np.ascontiguousarray(v) for name, v in inputs.items()}
    tables = [a[f"tbl_{f}"] for f in range(FIELDS)]
    vocab = [t.shape[0] for t in tables]
    starts = np.concatenate([[0], np.cumsum(vocab)])[:FIELDS]

    ids = np.zeros((BATCH, GROUPS * GROUP), np.int32)
    ids[:, :FIELDS] = a["ids"]
    ids = ids.reshape(TILES, TILE_B, GROUPS, GROUP).transpose(3, 1, 0, 2).reshape(P, TILES * GROUPS)
    base = np.zeros(GROUPS * GROUP, np.int32)
    base[:FIELDS] = starts
    base = np.repeat(base.reshape(GROUPS, GROUP).T, TILE_B, axis=0)

    w0 = a["L0_rec_w0"].reshape(FIELDS, FIELDS, UNITS)
    w0a, w0b = (np.zeros((WIDE, STEPS0, UNITS), np.float32) for _ in range(2))
    h = np.arange(FIELDS)
    for k, shifts in enumerate(SHIFT_OF):
        for j, s in enumerate(shifts):
            w0a[j * FIELDS:(j + 1) * FIELDS, k] = w0[h, (h + s) % FIELDS]
            w0b[j * FIELDS:(j + 1) * FIELDS, k] = w0[(h + s) % FIELDS, h]

    ins = {
        "ids": np.ascontiguousarray(ids), "base": np.ascontiguousarray(base), "table": np.concatenate(tables),
        "dense_t": np.ascontiguousarray(a["dense_ctx"].T), "w0a": w0a, "w0b": w0b,
        "w1": a["L0_rec_w1"], "w2": a["L0_rec_w2"], "b0": a["L0_rec_b0"], "b1": a["L0_rec_b1"],
        "b2": a["L0_rec_b2"], "wt1": a["W_top1"], "bt1": a["b_top1"], "wt2": a["W_top2"], "bt2": a["b_top2"],
        "wt3": a["W_top3"],
    }
    nc = bacc.Bacc("TRN2", target_bir_lowering=False, num_devices=1)
    t = {n: nc.dram_tensor(f"in_{n}", v.shape, mb.dt.from_np(v.dtype), kind="ExternalInput").ap()
         for n, v in ins.items()}
    xt = nc.dram_tensor("xt", [TILES, XT_ROWS, N], mb.dt.float32, kind="Internal").ap()
    out = nc.dram_tensor("out_y", [BATCH, 1], mb.dt.float32, kind="ExternalOutput").ap()
    build(nc, t["ids"], t["base"], t["table"], xt, t["dense_t"], t["w0a"], t["w0b"], t["w1"], t["w2"],
          t["b0"], t["b1"], t["b2"], t["wt1"], t["bt1"], t["wt2"], t["bt2"], t["wt3"], out)
    r = run(nc, [{f"in_{n}": v for n, v in ins.items()}], core_ids=[0])
    return r.results[0]["out_y"]
```
